# Optimizing a Trainium2 kernel written in Bass

```python
import numpy as np
import jax
import jax.numpy as jnp

def _softmax(x, axis=-1):
    return jax.nn.softmax(x, axis=axis)

def _gelu(x):
    return jax.nn.gelu(x, approximate=True)

def _silu(x):
    return jax.nn.silu(x)

def _sigmoid(x):
    return jax.nn.sigmoid(x)

def _layernorm(x, axis=-1, eps=1e-05):
    m = jnp.mean(x, axis=axis, keepdims=True)
    v = jnp.var(x, axis=axis, keepdims=True)
    return (x - m) / jnp.sqrt(v + eps)

def _scatter_add(tgt, idx, src, axis=0):
    return tgt.at[idx].add(src)

def _segment_sum(src, seg, n):
    return jax.ops.segment_sum(src, seg, n)
kernel_name = 'mk_dlrm_tower_d1_rec_r8_f5af3c'

def setup_inputs(seed: int=0):
    np.random.seed(seed)
    _w = jnp.asarray

    def _rec_inputs():
        import jax
        import jax.numpy as jnp
        _tk = jax.random.key(seed)
        dense_ctx = jax.random.normal(jax.random.fold_in(_tk, 190), (2048, 16), jnp.float32)
        ids = jnp.stack([jax.random.randint(jax.random.fold_in(_tk, 200 + f), (2048,), 0, v, jnp.int32) for f, v in enumerate([1000, 1250, 1000, 1000, 1250, 1250, 125000, 12500, 1250, 12500, 1250, 1250, 1250, 1250, 1250, 12500, 1000, 12500, 1000, 12500, 1000, 1250, 12500, 1000, 1000, 1000, 1000])], axis=1)
        tbl_0 = 0.05 * jax.random.normal(jax.random.fold_in(_tk, 500 + 0), (1000, 128), jnp.float32)
        tbl_1 = 0.05 * jax.random.normal(jax.random.fold_in(_tk, 500 + 1), (1250, 128), jnp.float32)
        tbl_2 = 0.05 * jax.random.normal(jax.random.fold_in(_tk, 500 + 2), (1000, 128), jnp.float32)
        tbl_3 = 0.05 * jax.random.normal(jax.random.fold_in(_tk, 500 + 3), (1000, 128), jnp.float32)
        tbl_4 = 0.05 * jax.random.normal(jax.random.fold_in(_tk, 500 + 4), (1250, 128), jnp.float32)
        tbl_5 = 0.05 * jax.random.normal(jax.random.fold_in(_tk, 500 + 5), (1250, 128), jnp.float32)
        tbl_6 = 0.05 * jax.random.normal(jax.random.fold_in(_tk, 500 + 6), (125000, 128), jnp.float32)
        tbl_7 = 0.05 * jax.random.normal(jax.random.fold_in(_tk, 500 + 7), (12500, 128), jnp.float32)
        tbl_8 = 0.05 * jax.random.normal(jax.random.fold_in(_tk, 500 + 8), (1250, 128), jnp.float32)
        tbl_9 = 0.05 * jax.random.normal(jax.random.fold_in(_tk, 500 + 9), (12500, 128), jnp.float32)
        tbl_10 = 0.05 * jax.random.normal(jax.random.fold_in(_tk, 500 + 10), (1250, 128), jnp.float32)
        tbl_11 = 0.05 * jax.random.normal(jax.random.fold_in(_tk, 500 + 11), (1250, 128), jnp.float32)
        tbl_12 = 0.05 * jax.random.normal(jax.random.fold_in(_tk, 500 + 12), (1250, 128), jnp.float32)
        tbl_13 = 0.05 * jax.random.normal(jax.random.fold_in(_tk, 500 + 13), (1250, 128), jnp.float32)
        tbl_14 = 0.05 * jax.random.normal(jax.random.fold_in(_tk, 500 + 14), (1250, 128), jnp.float32)
        tbl_15 = 0.05 * jax.random.normal(jax.random.fold_in(_tk, 500 + 15), (12500, 128), jnp.float32)
        tbl_16 = 0.05 * jax.random.normal(jax.random.fold_in(_tk, 500 + 16), (1000, 128), jnp.float32)
        tbl_17 = 0.05 * jax.random.normal(jax.random.fold_in(_tk, 500 + 17), (12500, 128), jnp.float32)
        tbl_18 = 0.05 * jax.random.normal(jax.random.fold_in(_tk, 500 + 18), (1000, 128), jnp.float32)
        tbl_19 = 0.05 * jax.random.normal(jax.random.fold_in(_tk, 500 + 19), (12500, 128), jnp.float32)
        tbl_20 = 0.05 * jax.random.normal(jax.random.fold_in(_tk, 500 + 20), (1000, 128), jnp.float32)
        tbl_21 = 0.05 * jax.random.normal(jax.random.fold_in(_tk, 500 + 21), (1250, 128), jnp.float32)
        tbl_22 = 0.05 * jax.random.normal(jax.random.fold_in(_tk, 500 + 22), (12500, 128), jnp.float32)
        tbl_23 = 0.05 * jax.random.normal(jax.random.fold_in(_tk, 500 + 23), (1000, 128), jnp.float32)
        tbl_24 = 0.05 * jax.random.normal(jax.random.fold_in(_tk, 500 + 24), (1000, 128), jnp.float32)
        tbl_25 = 0.05 * jax.random.normal(jax.random.fold_in(_tk, 500 + 25), (1000, 128), jnp.float32)
        tbl_26 = 0.05 * jax.random.normal(jax.random.fold_in(_tk, 500 + 26), (1000, 128), jnp.float32)
        _rk = jax.random.fold_in(_tk, 7)
        W_top1 = 0.0521996 * jax.random.normal(jax.random.fold_in(_tk, 801), (367, 512), jnp.float32)
        W_top2 = 0.0441942 * jax.random.normal(jax.random.fold_in(_tk, 802), (512, 256), jnp.float32)
        W_top3 = 0.0625 * jax.random.normal(jax.random.fold_in(_tk, 803), (256, 1), jnp.float32)
        b_top1 = jnp.zeros((512,), jnp.float32)
        b_top2 = jnp.zeros((256,), jnp.float32)
        return (dense_ctx, ids, tbl_0, tbl_1, tbl_2, tbl_3, tbl_4, tbl_5, tbl_6, tbl_7, tbl_8, tbl_9, tbl_10, tbl_11, tbl_12, tbl_13, tbl_14, tbl_15, tbl_16, tbl_17, tbl_18, tbl_19, tbl_20, tbl_21, tbl_22, tbl_23, tbl_24, tbl_25, tbl_26, W_top1, b_top1, W_top2, b_top2, W_top3)
    dense_ctx, ids, tbl_0, tbl_1, tbl_2, tbl_3, tbl_4, tbl_5, tbl_6, tbl_7, tbl_8, tbl_9, tbl_10, tbl_11, tbl_12, tbl_13, tbl_14, tbl_15, tbl_16, tbl_17, tbl_18, tbl_19, tbl_20, tbl_21, tbl_22, tbl_23, tbl_24, tbl_25, tbl_26, W_top1, b_top1, W_top2, b_top2, W_top3 = _rec_inputs()

    def _L0_rec_setup():
        import jax, jax.numpy as jnp
        import numpy as np

        def _tri_indices(num_feas):
            return np.array([i * num_feas + j for j in range(1, num_feas) for i in range(j)], dtype=np.int32)
        key = jax.random.key(seed)
        batch, num_feas, embed_dim = (2048, 27, 128)
        inputs = jax.random.normal(key, (batch, num_feas, embed_dim), dtype=jnp.float32)
        return {'inputs': inputs, 'num_feas': num_feas}
    _L0_rec_all = _L0_rec_setup()
    _L0_rec_in = {k: v for k, v in _L0_rec_all.items() if k in ()}
    del _L0_rec_all
    return {'dense_ctx': dense_ctx, 'ids': ids, 'tbl_0': tbl_0, 'tbl_1': tbl_1, 'tbl_2': tbl_2, 'tbl_3': tbl_3, 'tbl_4': tbl_4, 'tbl_5': tbl_5, 'tbl_6': tbl_6, 'tbl_7': tbl_7, 'tbl_8': tbl_8, 'tbl_9': tbl_9, 'tbl_10': tbl_10, 'tbl_11': tbl_11, 'tbl_12': tbl_12, 'tbl_13': tbl_13, 'tbl_14': tbl_14, 'tbl_15': tbl_15, 'tbl_16': tbl_16, 'tbl_17': tbl_17, 'tbl_18': tbl_18, 'tbl_19': tbl_19, 'tbl_20': tbl_20, 'tbl_21': tbl_21, 'tbl_22': tbl_22, 'tbl_23': tbl_23, 'tbl_24': tbl_24, 'tbl_25': tbl_25, 'tbl_26': tbl_26, 'W_top1': W_top1, 'b_top1': b_top1, 'W_top2': W_top2, 'b_top2': b_top2, 'W_top3': W_top3}

def reference(dense_ctx, ids, tbl_0, tbl_1, tbl_2, tbl_3, tbl_4, tbl_5, tbl_6, tbl_7, tbl_8, tbl_9, tbl_10, tbl_11, tbl_12, tbl_13, tbl_14, tbl_15, tbl_16, tbl_17, tbl_18, tbl_19, tbl_20, tbl_21, tbl_22, tbl_23, tbl_24, tbl_25, tbl_26, W_top1, b_top1, W_top2, b_top2, W_top3):
    import jax
    import jax.numpy as jnp

    def _L0_rec_ref(inputs, num_feas):
        import jax, jax.numpy as jnp
        import numpy as np

        def _tri_indices(num_feas):
            return np.array([i * num_feas + j for j in range(1, num_feas) for i in range(j)], dtype=np.int32)
        dot = jnp.einsum('bnd,bmd->bnm', inputs, inputs)
        idx = jnp.asarray(_tri_indices(num_feas))
        flat = dot.reshape(inputs.shape[0], num_feas * num_feas)
        return flat[:, idx]
    e = jnp.stack([tbl_0[ids[:, 0]], tbl_1[ids[:, 1]], tbl_2[ids[:, 2]], tbl_3[ids[:, 3]], tbl_4[ids[:, 4]], tbl_5[ids[:, 5]], tbl_6[ids[:, 6]], tbl_7[ids[:, 7]], tbl_8[ids[:, 8]], tbl_9[ids[:, 9]], tbl_10[ids[:, 10]], tbl_11[ids[:, 11]], tbl_12[ids[:, 12]], tbl_13[ids[:, 13]], tbl_14[ids[:, 14]], tbl_15[ids[:, 15]], tbl_16[ids[:, 16]], tbl_17[ids[:, 17]], tbl_18[ids[:, 18]], tbl_19[ids[:, 19]], tbl_20[ids[:, 20]], tbl_21[ids[:, 21]], tbl_22[ids[:, 22]], tbl_23[ids[:, 23]], tbl_24[ids[:, 24]], tbl_25[ids[:, 25]], tbl_26[ids[:, 26]]], axis=1)
    z = _L0_rec_ref(e, 27)
    z = z.reshape(z.shape[0], -1)
    h = jnp.concatenate([z, dense_ctx], axis=1)
    h = jnp.maximum(h @ W_top1 + b_top1, 0.0)
    h = jnp.maximum(h @ W_top2 + b_top2, 0.0)
    y = h @ W_top3
    return y

_drawn_inputs = setup_inputs


def setup_inputs(seed=0):
    import zlib

    import numpy as np

    out = dict(_drawn_inputs(seed))
    spreads = {'b_top1': (0.0, 0.1), 'b_top2': (0.0, 0.1)}
    factors = {}
    for name, (base, spread) in spreads.items():
        noise = np.random.default_rng([zlib.crc32(name.encode()), seed]).standard_normal(out[name].shape)
        drawn = base * np.exp(spread * noise) if base else spread * noise
        out[name] = jnp.asarray(drawn.astype(out[name].dtype))
    for name, factor in factors.items():
        out[name] = (out[name] * factor).astype(out[name].dtype)
    return out
```

```python
from contextlib import ExitStack

import numpy as np

import concourse.bass as bass
from concourse import mybir

F32 = mybir.dt.float32
BF16 = mybir.dt.bfloat16
F16 = mybir.dt.float16
I32 = mybir.dt.int32
ALU = mybir.AluOpType
ACT = mybir.ActivationFunctionType

P = 128
B, NF, D, CTX = 2048, 27, 128, 16
H1, H2 = 512, 256
TILES = 2
PAIRS = B // (TILES * P)
W = TILES * P
SIZES = [1000, 1250, 1000, 1000, 1250, 1250, 125000, 12500, 1250, 12500, 1250, 1250, 1250, 1250,
         1250, 12500, 1000, 12500, 1000, 12500, 1000, 1250, 12500, 1000, 1000, 1000, 1000]

MM_ROWS, CH = 1000, 8
MP = MM_ROWS // CH
NM = 8
MM_TABLES = [f for f in range(NF) if SIZES[f] == MM_ROWS][:NM]
GATHERED = [f for f in range(NF) if f not in MM_TABLES]
NG = len(GATHERED)
SLOTS = GATHERED + MM_TABLES
PARTS = 3

LOOK = NM // 2
TR = [range(a, min(a + 4, NG)) for a in range(0, NG, 4)]
NT = len(TR)
EMB_JOBS = LOOK + TILES * NT
Q, G = 4, 32
GS = 8
STEPS = G // GS
SHIFTS, RUN = NF // 2, 9
PAIRS_CH = SHIFTS * RUN
KCH = NF // RUN
CTX_CH = [P - PAIRS_CH, CTX - (P - PAIRS_CH), 0]
K1 = [PAIRS_CH + n for n in CTX_CH]
JEXT = NF + SHIFTS
SLOT = 32
MLP_JOBS = 6
BANKS = 2
N1, N2 = H1 // P, H2 // P


def first_layer_rows():
    rows = np.zeros((P, KCH), np.int32)
    for c in range(KCH):
        for s in range(1, SHIFTS + 1):
            for r in range(RUN):
                i = c * RUN + r
                a, b = sorted((SLOTS[i], SLOTS[(i + s) % NF]))
                rows[(s - 1) * RUN + r, c] = b * (b - 1) // 2 + a
        for k in range(CTX_CH[c]):
            rows[PAIRS_CH + k, c] = NF * (NF - 1) // 2 + sum(CTX_CH[:c]) + k
    return rows


def dlrm_tower(nc, ids, ids_mm, w1_rows, ident_in, dense_ctx, tables, W1, b1, W2, b2, W3, out):
    with ExitStack() as ctx:
        def sb(name, shape, dt):
            return ctx.enter_context(nc.sbuf_tensor(name, shape, dt))

        def ps(name, shape):
            return ctx.enter_context(nc.psum_tensor(name, shape, F32))

        def sem(name):
            return ctx.enter_context(nc.semaphore(name))

        ident = sb("ident", [P, P], F32)
        row_of = sb("row_of", [P, CH], F32)
        row_of_i = sb("row_of_i", [P, CH], I32)
        w1_idx = sb("w1_idx", [P, KCH], I32)
        w1_sb = sb("w1_sb", [P, KCH, H1], F32)
        w2_sb = sb("w2_sb", [P, N1, H2], F32)
        w3_sb = sb("w3_sb", [P, N2], F32)
        b1_sb = sb("b1_sb", [P, N1], F32)
        b2_sb = sb("b2_sb", [P, N2], F32)
        parts = sb("parts", [P, NM, PARTS, CH * D], BF16)
        stage = sb("stage", [P, 2, CH * D], F32)
        rest = sb("rest", [P, 2, CH * D], F32)
        idx = sb("idx", [P, TILES, NF], I32)
        rows = sb("rows", [P, TILES, NG, D], F32)
        ids_b = sb("ids_b", [P, NM, W], I32)
        ids_h = sb("ids_h", [P, NM, W], F16)
        onehot = sb("onehot", [P, NM, CH, W], BF16)
        embT = sb("embT", [P, TILES, P, SLOT], F32)
        blocks = sb("blocks", [P, TILES, NF, G], F32)
        turned = sb("turned", [P, TILES, JEXT * 32], F32)
        z = sb("z", [P, TILES, KCH, P], F32)
        zT = sb("zT", [P, KCH, W], F32)
        h1 = sb("h1", [P, N1, W], F32)
        h2 = sb("h2", [P, N2, W], F32)
        y = sb("y", [1, B], F32)

        emb_ps = [ps(f"emb_ps{k}", [P, 512]) for k in range(2)]
        gram_ps = [ps(f"gram_ps{k}", [P, 2, 512]) for k in range(2)]
        mlp_ps = [ps(f"mlp_ps{k}", [P, 512]) for k in range(2)]

        s_const = sem("s_const")
        s_w1idx = sem("s_w1idx")
        s_w1 = sem("s_w1")
        s_stage = [sem(f"s_stage{k}") for k in range(2)]
        s_part0 = sem("s_part0")
        s_rest = sem("s_rest")
        s_part1 = sem("s_part1")
        s_part2 = sem("s_part2")
        s_rowi = sem("s_rowi")
        s_row = sem("s_row")
        s_pad = sem("s_pad")
        s_idx = [sem(f"s_idx{t}") for t in range(TILES)]
        s_idsb = sem("s_idsb")
        s_ctx = sem("s_ctx")
        s_rows = [[sem(f"s_rows{t}_{k}") for k in range(NT)] for t in range(TILES)]
        pool_waited = sem("pool_waited")
        s_ids = sem("s_ids")
        s_onehot = sem("s_onehot")
        emb_filled = sem("emb_filled")
        emb_moved = sem("emb_moved")
        gram_filled = sem("gram_filled")
        gram_dve = sem("gram_dve")
        gram_act = sem("gram_act")
        s_turned = sem("s_turned")
        s_ext = sem("s_ext")
        s_z = sem("s_z")
        mlp_filled = sem("mlp_filled")
        mlp_moved = sem("mlp_moved")
        s_out = sem("s_out")

        def past(eng, s, value):
            if not (isinstance(value, int) and value <= 0):
                eng.wait_ge(s, value)

        def sweep(eng, body):
            body(0, True, False)
            with eng.Fori(1, PAIRS - 1) as p:
                body(p, False, False)
            body(PAIRS - 1, False, True)

        def sb_view(tile, first, dims, start=0, count=P):
            full = tile[:]
            pitch = full.ap[0][0]
            return bass.AP(full.tensor, start * pitch + first, [[pitch, count], *dims])

        block = ctx.enter_context(nc.Block())

        @block.sync
        def _(sp):
            def load_ids(p):
                src = ids_mm[:, bass.ts(p, W)]
                sp.dma_start(ids_b[:], src.partition_broadcast(P)).then_inc(s_idsb, 16)

            def load_idx(p, t):
                sp.dma_start(idx[:, t, :], ids[bass.ts(p * TILES + t, P), :]).then_inc(s_idx[t], 16)

            def load_table(k):
                src = tables[MM_TABLES[k]].rearrange("(p c) d -> p (c d)", c=CH)
                sp.dma_start(stage[0:MP, k % 2, :], src).then_inc(s_stage[k % 2], 16)

            def store_y(p):
                sp.dma_start(out[bass.ts(p, W), :].rearrange("n o -> o n"), y[:, bass.ts(p, W)]).then_inc(s_out, 16)

            load_idx(0, 0)
            load_idx(0, 1)
            load_ids(0)
            load_table(0)
            load_table(1)
            sp.dma_start(ident[:], ident_in).then_inc(s_const, 16)
            sp.dma_start(w1_idx[:], w1_rows).then_inc(s_w1idx, 16)
            sp.dma_start(w2_sb[:], W2.rearrange("(k p) n -> p k n", p=P)).then_inc(s_const, 16)
            with nc.allow_non_contiguous_dma(reason="short vectors, once"):
                sp.dma_start(w3_sb[:], W3.rearrange("(k p) n -> p (k n)", p=P)).then_inc(s_const, 16)
                sp.dma_start(b1_sb[:], b1.rearrange("(k p) -> p k", p=P)).then_inc(s_const, 16)
                sp.dma_start(b2_sb[:], b2.rearrange("(k p) -> p k", p=P)).then_inc(s_const, 16)
            for k in range(2, NM):
                sp.wait_ge(s_rest, k - 1)
                sp.wait_ge(s_part0, k - 1)
                load_table(k)

            def body(p, first, last):
                if first:
                    sp.wait_ge(s_pad, 2)
                past(sp, mlp_filled, (p - 1) * MLP_JOBS + TILES)
                src = dense_ctx[bass.ts(p, W), :].rearrange("(t p) c -> p t c", p=P)
                for c in range(KCH):
                    if CTX_CH[c]:
                        at = sum(CTX_CH[:c])
                        sp.dma_start(z[:, :, c, PAIRS_CH:PAIRS_CH + CTX_CH[c]], src[:, :, at:at + CTX_CH[c]]
                                     ).then_inc(s_ctx, 16)
                if not last:
                    sp.wait_ge(s_ids, p + 1)
                    load_ids(p + 1)
                    for t in range(TILES):
                        sp.wait_ge(emb_filled, p * EMB_JOBS + LOOK + (t + 1) * NT)
                        load_idx(p + 1, t)
                if not first:
                    sp.wait_ge(mlp_moved, BANKS + p * MLP_JOBS)
                    store_y(p - 1)

            sweep(sp, body)
            sp.wait_ge(mlp_moved, BANKS + PAIRS * MLP_JOBS)
            store_y(PAIRS - 1)
            sp.wait_ge(s_out, PAIRS * 16)

        @block.gpsimd
        def _(pool):
            pool.iota(row_of_i[:], [[1, CH]], base=0, channel_multiplier=CH).then_inc(s_rowi, 1)

            def load_w1():
                pool.wait_ge(s_w1idx, 16)
                for c in range(KCH):
                    n = K1[c]
                    pool.indirect_dma_start(w1_sb[0:n, c, :], None, W1,
                                            bass.IndirectOffsetOnAxis(w1_idx[0:n, c:c + 1], 0)
                                            ).then_inc(s_w1, 16)

            def body(p, first, last):
                for t in range(TILES):
                    pool.wait_ge(s_idx[t], (p + 1) * 16)
                    for k in range(NT):
                        past(pool, emb_filled, (p - 1) * EMB_JOBS + LOOK + t * NT + k + 1)
                        pool.sem_inc(pool_waited, 1)
                        for n in TR[k]:
                            f = GATHERED[n]
                            pool.indirect_dma_start(rows[:, t, n, :], None, tables[f],
                                                    bass.IndirectOffsetOnAxis(idx[:, t, f:f + 1], 0)
                                                    ).then_inc(s_rows[t][k], 16)
                if first:
                    load_w1()

            sweep(pool, body)

        @block.scalar
        def _(act):
            def split_first(k):
                act.wait_ge(s_stage[k % 2], 16 * (k // 2 + 1))
                nc.scalar.activation(parts[0:MP, k, 0, :], stage[0:MP, k % 2, :], ACT.Copy).then_inc(s_part0, 1)

            def split_second(k):
                act.wait_ge(s_rest, k + 1)
                nc.scalar.activation(parts[0:MP, k, 1, :], rest[0:MP, k % 2, :], ACT.Copy).then_inc(s_part1, 1)

            def move_lookup(p, k):
                job = p * EMB_JOBS + k
                act.wait_ge(emb_filled, job + 1)
                dst = sb_view(embT, NG + 2 * k, [[1, 2], [SLOT, W]])
                src = emb_ps[k % 2][:].rearrange("d (f b) -> d f b", f=2)
                nc.scalar.activation(dst, src, ACT.Copy).then_inc(emb_moved, 1)

            def move_rows(p, t, k):
                n = len(TR[k])
                job = LOOK + t * NT + k
                act.wait_ge(emb_filled, p * EMB_JOBS + job + 1)
                dst = sb_view(embT, t * P * SLOT + TR[k][0], [[1, n], [SLOT, P]])
                src = emb_ps[job % 2][:, 0:n * P].rearrange("d (f b) -> d f b", f=n)
                nc.scalar.activation(dst, src, ACT.Copy).then_inc(emb_moved, 1)

            def move_z(p, t):
                act.wait_ge(mlp_filled, p * MLP_JOBS + t + 1)
                nc.scalar.activation(zT[:, :, t * P:(t + 1) * P],
                                     mlp_ps[t][:, 0:KCH * P].rearrange("k (c b) -> k c b", c=KCH),
                                     ACT.Copy).then_inc(mlp_moved, 1)

            def bias_relu(dst, bias, p, job, ns):
                act.wait_ge(mlp_filled, p * MLP_JOBS + job + 1)
                for m, n in enumerate(ns):
                    last = nc.scalar.activation(dst[:, n, :], mlp_ps[job % 2][:, m * W:(m + 1) * W], ACT.Relu,
                                                bias=bias[:, n:n + 1])
                last.then_inc(mlp_moved, 1)

            def move_y(p):
                act.wait_ge(mlp_filled, (p + 1) * MLP_JOBS)
                nc.scalar.activation(y[:, bass.ts(p, W)], mlp_ps[1][0:1, 0:W], ACT.Copy).then_inc(mlp_moved, 1)

            def keep_blocks(p, t, s):
                step = t * STEPS + s
                act.wait_ge(gram_filled, p * TILES * STEPS + step + 1)
                past(act, s_turned, (p - 1) * TILES + t + 1)
                for q in range(Q):
                    src = gram_ps[1][q * 32:(q + 1) * 32, :, 0:4 * Q * NF].rearrange(
                        "i h (g c) -> i h g c", g=4)[:, :, :, q * NF:(q + 1) * NF]
                    dst = sb_view(blocks, t * NF * G + GS * s, [[4, 2], [1, 4], [G, NF]], q * 32, 32)
                    last = nc.scalar.activation(dst, src, ACT.Copy)
                last.then_inc(gram_act, 1)

            def layers(p, step):
                if step == 0:
                    move_z(p, 0)
                    move_z(p, 1)
                elif step == 1:
                    act.wait_ge(s_const, 16 * 5)
                    bias_relu(h1, b1_sb, p, 2, (0, 1))
                    bias_relu(h1, b1_sb, p, 3, (2, 3))
                elif step == 2:
                    bias_relu(h2, b2_sb, p, 4, (0, 1))
                else:
                    move_y(p)

            act.sem_inc(mlp_moved, BANKS)
            split_first(0)
            for k in range(NM):
                if k + 1 < NM:
                    split_first(k + 1)
                split_second(k)
                if k >= 5 and k % 2:
                    move_lookup(0, (k - 5) // 2)

            def body(p, first, last):
                for k in range(LOOK):
                    if not first:
                        layers(p - 1, k)
                    if not (first and k <= (NM - 6) // 2):
                        move_lookup(p, k)
                for t in range(TILES):
                    for k in range(NT):
                        move_rows(p, t, k)
                    for s in range(1, STEPS, 2):
                        keep_blocks(p, t, s)

            sweep(act, body)
            for k in range(LOOK):
                layers(PAIRS - 1, k)

        @block.vector
        def _(dve):
            def split_rest(k):
                dve.wait_ge(s_stage[k % 2], 16 * (k // 2 + 1))
                dve.wait_ge(s_part0, k + 1)
                if k >= 2:
                    dve.wait_ge(s_part2, k - 1)
                    dve.wait_ge(s_part1, k - 1)
                nc.vector.tensor_tensor(rest[0:MP, k % 2, :], stage[0:MP, k % 2, :], parts[0:MP, k, 0, :],
                                        ALU.subtract).then_inc(s_rest, 1)

            def split_third(k):
                dve.wait_ge(s_part1, k + 1)
                dve.wait_ge(s_rest, k + 1)
                nc.vector.tensor_tensor(parts[0:MP, k, 2, :], rest[0:MP, k % 2, :], parts[0:MP, k, 1, :],
                                        ALU.subtract).then_inc(s_part2, 1)

            def convert_ids(p):
                dve.wait_ge(s_idsb, (p + 1) * 16)
                nc.vector.tensor_copy(ids_h[:], ids_b[:]).then_inc(s_ids, 1)
                dve.wait_ge(s_ids, p + 1)

            def make_onehot(p, k):
                past(dve, emb_filled, (p - 1) * EMB_JOBS + k // 2 + 1)
                for c in range(CH):
                    last = nc.vector.tensor_scalar(onehot[:, k, c, :], ids_h[:, k, :], row_of[:, c:c + 1], None,
                                                   ALU.is_equal)
                last.then_inc(s_onehot, 1)

            def keep_blocks(p, t, s):
                step = t * STEPS + s
                dve.wait_ge(gram_filled, p * TILES * STEPS + step + 1)
                for q in range(Q):
                    src = gram_ps[0][q * 32:(q + 1) * 32, :, 0:4 * Q * NF].rearrange(
                        "i h (g c) -> i h g c", g=4)[:, :, :, q * NF:(q + 1) * NF]
                    dst = sb_view(blocks, t * NF * G + GS * s, [[4, 2], [1, 4], [G, NF]], q * 32, 32)
                    last = nc.vector.tensor_copy(dst, src)
                last.then_inc(gram_dve, 1)

            def turn(p, t):
                dve.wait_ge(gram_dve, (p * TILES + t + 1) * (STEPS // 2))
                dve.wait_ge(gram_act, (p * TILES + t + 1) * (STEPS // 2))
                past(dve, s_z, (p - 1) * TILES + t + 1)
                nc.vector.transpose(turned[:, t, 0:NF * G], blocks[:, t, :, :].rearrange("p j g -> p (j g)")
                                    ).then_inc(s_turned, 1)
                dve.wait_ge(s_turned, p * TILES + t + 1)
                nc.vector.tensor_copy(turned[:, t, NF * 32:], turned[:, t, 0:SHIFTS * 32]).then_inc(s_ext, 1)
                dve.wait_ge(s_ext, p * TILES + t + 1)
                past(dve, mlp_filled, (p - 1) * MLP_JOBS + t + 1)
                src = sb_view(turned, t * JEXT * 32 + 32, [[33 * RUN, KCH], [32, SHIFTS], [33, RUN]])
                dst = z[:, t, :, 0:PAIRS_CH].rearrange("b c (s r) -> b c s r", r=RUN)
                nc.vector.tensor_copy(dst, src).then_inc(s_z, 1)

            dve.memset(embT[:, :, :, NF:], 0.0).then_inc(s_pad, 1)
            dve.memset(z[:, :, 1:, PAIRS_CH:], 0.0).then_inc(s_pad, 1)
            dve.wait_ge(s_rowi, 1)
            nc.vector.tensor_copy(row_of[:], row_of_i[:]).then_inc(s_row, 1)
            convert_ids(0)
            dve.wait_ge(s_row, 1)
            split_rest(0)
            for k in range(NM):
                if k + 1 < NM:
                    split_rest(k + 1)
                split_third(k)
                make_onehot(0, k)

            def body(p, first, last):
                for t in range(TILES):
                    for s in range(0, STEPS, 2):
                        keep_blocks(p, t, s)
                    turn(p, t)
                    if t == 0 and not last:
                        convert_ids(p + 1)
                        for k in range(NM):
                            make_onehot(p + 1, k)

            sweep(dve, body)

        @block.tensor
        def _(pe):
            def lookup(p, k):
                past(pe, emb_moved, p * EMB_JOBS + k - 1)
                for m in range(2):
                    f = 2 * k + m
                    pe.wait_ge(s_onehot, p * NM + f + 1)
                    if isinstance(p, int) and p == 0:
                        pe.wait_ge(s_part2, f + 1)
                        pe.wait_ge(s_part1, f + 1)
                    for c in range(CH):
                        for part in range(PARTS):
                            last = nc.tensor.matmul(emb_ps[k % 2][:, m * W:(m + 1) * W],
                                                    parts[0:MP, f, part, c * D:(c + 1) * D],
                                                    onehot[0:MP, f, c, :],
                                                    start=(c == 0 and part == 0),
                                                    stop=(c == CH - 1 and part == PARTS - 1))
                last.then_inc(emb_filled, 1)

            def transpose_rows(p, t, k):
                job = LOOK + t * NT + k
                past(pe, emb_moved, p * EMB_JOBS + job - 1)
                pe.wait_ge(s_rows[t][k], (p + 1) * 16 * len(TR[k]))
                for m, n in enumerate(TR[k]):
                    last = nc.tensor.transpose(emb_ps[job % 2][:, m * P:(m + 1) * P], rows[:, t, n, :], ident[:])
                last.then_inc(emb_filled, 1)

            def gram(p, t, s):
                step = t * STEPS + s
                past(pe, (gram_dve, gram_act)[s % 2], p * (TILES * STEPS // 2) + step // 2)
                for g in range(GS):
                    four = embT[:, t, (GS * s + g) * Q:(GS * s + g + 1) * Q, :]
                    last = nc.tensor.matmul(gram_ps[s % 2][:, g // 4, (g % 4) * Q * NF:(g % 4 + 1) * Q * NF],
                                            four.rearrange("d q f -> d (q f)"), four[:, :, 0:NF],
                                            start=True, stop=True)
                last.then_inc(gram_filled, 1)

            def transpose_z(p, t):
                pe.wait_ge(s_z, p * TILES + t + 1)
                pe.wait_ge(s_ctx, (p + 1) * 16 * sum(n > 0 for n in CTX_CH))
                pe.wait_ge(mlp_moved, p * MLP_JOBS + t + 1)
                for c in range(KCH):
                    last = nc.tensor.transpose(mlp_ps[t][:, c * P:(c + 1) * P], z[:, t, c, :], ident[:])
                last.then_inc(mlp_filled, 1)

            def layers(p, step):
                base = p * MLP_JOBS
                if step == 0:
                    transpose_z(p, 0)
                    transpose_z(p, 1)
                elif step == 1:
                    pe.wait_ge(s_w1, 16 * KCH)
                    pe.wait_ge(s_const, 16 * 5)
                    for job in (2, 3):
                        pe.wait_ge(mlp_moved, BANKS + base + 2)
                        for m in range(2):
                            n = 2 * (job - 2) + m
                            for c in range(KCH):
                                last = nc.tensor.matmul(mlp_ps[job % 2][:, m * W:(m + 1) * W],
                                                        w1_sb[0:K1[c], c, n * P:(n + 1) * P], zT[0:K1[c], c, :],
                                                        start=(c == 0), stop=(c == KCH - 1))
                        last.then_inc(mlp_filled, 1)
                elif step == 2:
                    pe.wait_ge(mlp_moved, BANKS + base + 4)
                    for m in range(N2):
                        for n in range(N1):
                            last = nc.tensor.matmul(mlp_ps[0][:, m * W:(m + 1) * W],
                                                    w2_sb[:, n, m * P:(m + 1) * P], h1[:, n, :],
                                                    start=(n == 0), stop=(n == N1 - 1))
                    last.then_inc(mlp_filled, 1)
                else:
                    pe.wait_ge(mlp_moved, BANKS + base + 5)
                    for m in range(N2):
                        last = nc.tensor.matmul(mlp_ps[1][0:1, 0:W], w3_sb[:, m:m + 1], h2[:, m, :],
                                                start=(m == 0), stop=(m == N2 - 1))
                    last.then_inc(mlp_filled, 1)

            pe.wait_ge(s_const, 16 * 5)
            pe.wait_ge(s_pad, 1)

            def body(p, first, last):
                for k in range(LOOK):
                    if not first:
                        layers(p - 1, k)
                    lookup(p, k)
                for t in range(TILES):
                    for k in range(NT):
                        transpose_rows(p, t, k)
                    pe.wait_ge(emb_moved, p * EMB_JOBS + LOOK + (t + 1) * NT)
                    for s in range(STEPS):
                        gram(p, t, s)

            sweep(pe, body)
            for k in range(LOOK):
                layers(PAIRS - 1, k)


def kernel(**inputs):
    import concourse.bacc as bacc
    from concourse.bass_utils import run_bass_kernel_spmd

    nc = bacc.Bacc("TRN2", target_bir_lowering=False, num_devices=1)
    arrays = {}

    def give(name, a):
        a = np.ascontiguousarray(a)
        arrays[name] = a
        return nc.dram_tensor(name, a.shape, mybir.dt.from_np(a.dtype), kind="ExternalInput").ap()

    ids_in = np.asarray(inputs["ids"]).reshape(B // P, Q, G, NF).transpose(0, 2, 1, 3).reshape(B, NF)
    ids = give("in_ids", ids_in)
    ids_mm = give("in_ids_mm", ids_in[:, MM_TABLES].T)
    w1_rows = give("in_w1_rows", first_layer_rows())
    ident = give("in_ident", np.eye(P, dtype=np.float32))
    dense_ctx = give("in_dense_ctx", inputs["dense_ctx"])
    tables = [give(f"in_tbl_{f}", inputs[f"tbl_{f}"]) for f in range(NF)]
    W1, b1, W2, b2, W3 = (give(f"in_{n}", inputs[n]) for n in ("W_top1", "b_top1", "W_top2", "b_top2", "W_top3"))
    out = nc.dram_tensor("out", (B, 1), F32, kind="ExternalOutput").ap()
    dlrm_tower(nc, ids, ids_mm, w1_rows, ident, dense_ctx, tables, W1, b1, W2, b2, W3, out)
    r = run_bass_kernel_spmd(nc, [arrays], core_ids=[0])
    return r.results[0]["out"]
```

```python
from contextlib import ExitStack

import numpy as np

import concourse.bass as bass
from concourse import mybir

F32 = mybir.dt.float32
BF16 = mybir.dt.bfloat16
F16 = mybir.dt.float16
I32 = mybir.dt.int32
ALU = mybir.AluOpType
ACT = mybir.ActivationFunctionType

P = 128
B, NF, D, CTX = 2048, 27, 128, 16
H1, H2 = 512, 256
TILES = 2
PAIRS = B // (TILES * P)
W = TILES * P
SIZES = [1000, 1250, 1000, 1000, 1250, 1250, 125000, 12500, 1250, 12500, 1250, 1250, 1250, 1250,
         1250, 12500, 1000, 12500, 1000, 12500, 1000, 1250, 12500, 1000, 1000, 1000, 1000]

MM_ROWS, CH = 1000, 8
MP = MM_ROWS // CH
NM = 6
MM_TABLES = [f for f in range(NF) if SIZES[f] == MM_ROWS][:NM]
GATHERED = [f for f in range(NF) if f not in MM_TABLES]
NG = len(GATHERED)
SLOTS = GATHERED + MM_TABLES
PARTS = 3

LOOK = 4
LK = [range(-(-NM * k // LOOK), -(-NM * (k + 1) // LOOK)) for k in range(LOOK)]
JOB_OF = {f: k for k in range(LOOK) for f in LK[k]}
TR = [range(a, min(a + 4, NG)) for a in range(0, NG, 4)]
NT = len(TR)
EMB_JOBS = LOOK + TILES * NT
Q, G = 4, 32
GS = 8
STEPS = G // GS
SHIFTS, RUN = NF // 2, 9
PAIRS_CH = SHIFTS * RUN
KCH = NF // RUN
CTX_CH = [P - PAIRS_CH, CTX - (P - PAIRS_CH), 0]
K1 = [PAIRS_CH + n for n in CTX_CH]
JEXT = NF + SHIFTS
SLOT = 32
MLP_JOBS = 6
BANKS = 2
N1, N2 = H1 // P, H2 // P


def first_layer_rows():
    rows = np.zeros((P, KCH), np.int32)
    for c in range(KCH):
        for s in range(1, SHIFTS + 1):
            for r in range(RUN):
                i = c * RUN + r
                a, b = sorted((SLOTS[i], SLOTS[(i + s) % NF]))
                rows[(s - 1) * RUN + r, c] = b * (b - 1) // 2 + a
        for k in range(CTX_CH[c]):
            rows[PAIRS_CH + k, c] = NF * (NF - 1) // 2 + sum(CTX_CH[:c]) + k
    return rows


def dlrm_tower(nc, ids, ids_mm, w1_rows, ident_in, dense_ctx, tables, W1, b1, W2, b2, W3, out):
    with ExitStack() as ctx:
        def sb(name, shape, dt):
            return ctx.enter_context(nc.sbuf_tensor(name, shape, dt))

        def ps(name, shape):
            return ctx.enter_context(nc.psum_tensor(name, shape, F32))

        def sem(name):
            return ctx.enter_context(nc.semaphore(name))

        ident = sb("ident", [P, P], F32)
        row_of = sb("row_of", [P, CH], F32)
        row_of_i = sb("row_of_i", [P, CH], I32)
        w1_idx = sb("w1_idx", [P, KCH], I32)
        w1_sb = sb("w1_sb", [P, KCH, H1], F32)
        w2_sb = sb("w2_sb", [P, N1, H2], F32)
        w3_sb = sb("w3_sb", [P, N2], F32)
        b1_sb = sb("b1_sb", [P, N1], F32)
        b2_sb = sb("b2_sb", [P, N2], F32)
        parts = sb("parts", [P, NM, PARTS, CH * D], BF16)
        stage = sb("stage", [P, 2, CH * D], F32)
        rest = sb("rest", [P, 2, CH * D], F32)
        idx = sb("idx", [P, TILES, NF], I32)
        rows = sb("rows", [P, TILES, NG, D], F32)
        ids_b = sb("ids_b", [P, NM, W], I32)
        ids_h = sb("ids_h", [P, NM, W], F16)
        onehot = sb("onehot", [P, NM, CH, W], BF16)
        embT = sb("embT", [P, TILES, P, SLOT], F32)
        blocks = sb("blocks", [P, TILES, NF, G], F32)
        turned = sb("turned", [P, TILES, JEXT * 32], F32)
        z = sb("z", [P, TILES, KCH, P], F32)
        zT = sb("zT", [P, KCH, W], F32)
        h1 = sb("h1", [P, N1, W], F32)
        h2 = sb("h2", [P, N2, W], F32)
        y = sb("y", [1, B], F32)

        emb_ps = [ps(f"emb_ps{k}", [P, 512]) for k in range(2)]
        gram_ps = [ps(f"gram_ps{k}", [P, 2, 512]) for k in range(2)]
        mlp_ps = [ps(f"mlp_ps{k}", [P, 512]) for k in range(2)]

        s_const = sem("s_const")
        s_w1idx = sem("s_w1idx")
        s_w1 = sem("s_w1")
        s_stage = [sem(f"s_stage{k}") for k in range(2)]
        s_part0 = sem("s_part0")
        s_rest = sem("s_rest")
        s_part1 = sem("s_part1")
        s_part2 = sem("s_part2")
        s_rowi = sem("s_rowi")
        s_row = sem("s_row")
        s_pad = sem("s_pad")
        s_idx = [sem(f"s_idx{t}") for t in range(TILES)]
        s_idsb = sem("s_idsb")
        s_ctx = sem("s_ctx")
        s_rows = [[sem(f"s_rows{t}_{k}") for k in range(NT)] for t in range(TILES)]
        pool_waited = sem("pool_waited")
        s_ids = sem("s_ids")
        s_onehot = sem("s_onehot")
        emb_filled = sem("emb_filled")
        emb_act = sem("emb_act")
        emb_dve = sem("emb_dve")
        gram_filled = sem("gram_filled")
        gram_dve = sem("gram_dve")
        gram_act = sem("gram_act")
        s_turned = sem("s_turned")
        s_ext = sem("s_ext")
        s_z = sem("s_z")
        mlp_filled = sem("mlp_filled")
        mlp_moved = sem("mlp_moved")
        s_out = sem("s_out")

        def past(eng, s, value):
            if not (isinstance(value, int) and value <= 0):
                eng.wait_ge(s, value)

        def sweep(eng, body):
            body(0, True, False)
            with eng.Fori(1, PAIRS - 1) as p:
                body(p, False, False)
            body(PAIRS - 1, False, True)

        def sb_view(tile, first, dims, start=0, count=P):
            full = tile[:]
            pitch = full.ap[0][0]
            return bass.AP(full.tensor, start * pitch + first, [[pitch, count], *dims])

        def lookup_views(k):
            n = len(LK[k])
            return (sb_view(embT, NG + LK[k][0], [[1, n], [SLOT, W]]),
                    emb_ps[k % 2][:, 0:n * W].rearrange("d (f b) -> d f b", f=n))

        def row_views(t, k):
            n = len(TR[k])
            return (sb_view(embT, t * P * SLOT + TR[k][0], [[1, n], [SLOT, P]]),
                    emb_ps[(LOOK + t * NT + k) % 2][:, 0:n * P].rearrange("d (f b) -> d f b", f=n))

        def block_views(t, s, q):
            src = gram_ps[s % 2][q * 32:(q + 1) * 32, :, 0:4 * Q * NF].rearrange("i h (g c) -> i h g c", g=4)
            return (sb_view(blocks, t * NF * G + GS * s, [[4, 2], [1, 4], [G, NF]], q * 32, 32),
                    src[:, :, :, q * NF:(q + 1) * NF])

        block = ctx.enter_context(nc.Block())

        @block.sync
        def _(sp):
            def load_ids(p):
                src = ids_mm[:, bass.ts(p, W)]
                sp.dma_start(ids_b[:], src.partition_broadcast(P)).then_inc(s_idsb, 16)

            def load_idx(p, t):
                sp.dma_start(idx[:, t, :], ids[bass.ts(p * TILES + t, P), :]).then_inc(s_idx[t], 16)

            def load_table(k):
                src = tables[MM_TABLES[k]].rearrange("(p c) d -> p (c d)", c=CH)
                sp.dma_start(stage[0:MP, k % 2, :], src).then_inc(s_stage[k % 2], 16)

            def store_y(p):
                sp.dma_start(out[bass.ts(p, W), :].rearrange("n o -> o n"), y[:, bass.ts(p, W)]).then_inc(s_out, 16)

            load_idx(0, 0)
            load_idx(0, 1)
            load_ids(0)
            load_table(0)
            load_table(1)
            sp.dma_start(ident[:], ident_in).then_inc(s_const, 16)
            sp.dma_start(w1_idx[:], w1_rows).then_inc(s_w1idx, 16)
            sp.dma_start(w2_sb[:], W2.rearrange("(k p) n -> p k n", p=P)).then_inc(s_const, 16)
            with nc.allow_non_contiguous_dma(reason="short vectors, once"):
                sp.dma_start(w3_sb[:], W3.rearrange("(k p) n -> p (k n)", p=P)).then_inc(s_const, 16)
                sp.dma_start(b1_sb[:], b1.rearrange("(k p) -> p k", p=P)).then_inc(s_const, 16)
                sp.dma_start(b2_sb[:], b2.rearrange("(k p) -> p k", p=P)).then_inc(s_const, 16)
            for k in range(2, NM):
                sp.wait_ge(s_rest, k - 1)
                sp.wait_ge(s_part0, k - 1)
                load_table(k)

            def body(p, first, last):
                if not last:
                    sp.wait_ge(s_ids, p + 1)
                    load_ids(p + 1)
                if first:
                    sp.wait_ge(s_pad, 2)
                past(sp, mlp_filled, (p - 1) * MLP_JOBS + TILES)
                src = dense_ctx[bass.ts(p, W), :].rearrange("(t p) c -> p t c", p=P)
                for c in range(KCH):
                    if CTX_CH[c]:
                        at = sum(CTX_CH[:c])
                        sp.dma_start(z[:, :, c, PAIRS_CH:PAIRS_CH + CTX_CH[c]], src[:, :, at:at + CTX_CH[c]]
                                     ).then_inc(s_ctx, 16)
                if not last:
                    for t in range(TILES):
                        sp.wait_ge(emb_filled, p * EMB_JOBS + LOOK + (t + 1) * NT)
                        load_idx(p + 1, t)
                if not first:
                    sp.wait_ge(mlp_moved, BANKS + p * MLP_JOBS)
                    store_y(p - 1)

            sweep(sp, body)
            sp.wait_ge(mlp_moved, BANKS + PAIRS * MLP_JOBS)
            store_y(PAIRS - 1)
            sp.wait_ge(s_out, PAIRS * 16)

        @block.gpsimd
        def _(pool):
            pool.iota(row_of_i[:], [[1, CH]], base=0, channel_multiplier=CH).then_inc(s_rowi, 1)

            def load_w1():
                pool.wait_ge(s_w1idx, 16)
                for c in range(KCH):
                    n = K1[c]
                    pool.indirect_dma_start(w1_sb[0:n, c, :], None, W1,
                                            bass.IndirectOffsetOnAxis(w1_idx[0:n, c:c + 1], 0)
                                            ).then_inc(s_w1, 16)

            def body(p, first, last):
                for t in range(TILES):
                    pool.wait_ge(s_idx[t], (p + 1) * 16)
                    for k in range(NT):
                        past(pool, emb_filled, (p - 1) * EMB_JOBS + LOOK + t * NT + k + 1)
                        pool.sem_inc(pool_waited, 1)
                        for n in TR[k]:
                            f = GATHERED[n]
                            pool.indirect_dma_start(rows[:, t, n, :], None, tables[f],
                                                    bass.IndirectOffsetOnAxis(idx[:, t, f:f + 1], 0)
                                                    ).then_inc(s_rows[t][k], 16)
                if first:
                    load_w1()

            sweep(pool, body)

        @block.scalar
        def _(act):
            def split_first(k):
                act.wait_ge(s_stage[k % 2], 16 * (k // 2 + 1))
                nc.scalar.activation(parts[0:MP, k, 0, :], stage[0:MP, k % 2, :], ACT.Copy).then_inc(s_part0, 1)

            def split_second(k):
                act.wait_ge(s_rest, k + 1)
                nc.scalar.activation(parts[0:MP, k, 1, :], rest[0:MP, k % 2, :], ACT.Copy).then_inc(s_part1, 1)

            def move_lookup(p, k):
                act.wait_ge(emb_filled, p * EMB_JOBS + k + 1)
                nc.scalar.activation(*lookup_views(k), ACT.Copy).then_inc(emb_act, 1)

            def move_rows(p, t, k):
                act.wait_ge(emb_filled, p * EMB_JOBS + LOOK + t * NT + k + 1)
                nc.scalar.activation(*row_views(t, k), ACT.Copy).then_inc(emb_act, 1)

            def move_z(p, t):
                act.wait_ge(mlp_filled, p * MLP_JOBS + t + 1)
                nc.scalar.activation(zT[:, :, t * P:(t + 1) * P],
                                     mlp_ps[t][:, 0:KCH * P].rearrange("k (c b) -> k c b", c=KCH),
                                     ACT.Copy).then_inc(mlp_moved, 1)

            def bias_relu(dst, bias, p, job, ns):
                act.wait_ge(mlp_filled, p * MLP_JOBS + job + 1)
                for m, n in enumerate(ns):
                    last = nc.scalar.activation(dst[:, n, :], mlp_ps[job % 2][:, m * W:(m + 1) * W], ACT.Relu,
                                                bias=bias[:, n:n + 1])
                last.then_inc(mlp_moved, 1)

            def move_y(p):
                act.wait_ge(mlp_filled, (p + 1) * MLP_JOBS)
                nc.scalar.activation(y[:, bass.ts(p, W)], mlp_ps[1][0:1, 0:W], ACT.Copy).then_inc(mlp_moved, 1)

            def keep_blocks(p, t, s):
                step = t * STEPS + s
                act.wait_ge(gram_filled, p * TILES * STEPS + step + 1)
                past(act, s_turned, (p - 1) * TILES + t + 1)
                for q in range(Q):
                    last = nc.scalar.activation(*block_views(t, s, q), ACT.Copy)
                last.then_inc(gram_act, 1)

            def layers(p, step):
                if step == 0:
                    move_z(p, 1)
                elif step == 1:
                    act.wait_ge(s_const, 16 * 5)
                    bias_relu(h1, b1_sb, p, 2, (0, 1))
                    bias_relu(h1, b1_sb, p, 3, (2, 3))
                elif step == 2:
                    bias_relu(h2, b2_sb, p, 4, (0, 1))
                else:
                    move_y(p)

            act.sem_inc(mlp_moved, BANKS)
            split_first(0)
            for k in range(NM):
                if k + 1 < NM:
                    split_first(k + 1)
                split_second(k)
                if k == NM - 2:
                    move_lookup(0, 0)

            def body(p, first, last):
                for k in range(LOOK):
                    if k % 2 == 0 and not (first and k == 0):
                        move_lookup(p, k)
                    if not first and k < 3:
                        layers(p - 1, k)
                for t in range(TILES):
                    for k in range(NT):
                        if (LOOK + t * NT + k) % 2 == 0:
                            move_rows(p, t, k)
                    if t == 0 and not first:
                        layers(p - 1, 3)
                    for s in range(1, STEPS, 2):
                        keep_blocks(p, t, s)
                move_z(p, 0)

            sweep(act, body)
            for k in range(4):
                layers(PAIRS - 1, k)

        @block.vector
        def _(dve):
            def split_rest(k):
                dve.wait_ge(s_stage[k % 2], 16 * (k // 2 + 1))
                dve.wait_ge(s_part0, k + 1)
                if k >= 2:
                    dve.wait_ge(s_part2, k - 1)
                    dve.wait_ge(s_part1, k - 1)
                nc.vector.tensor_tensor(rest[0:MP, k % 2, :], stage[0:MP, k % 2, :], parts[0:MP, k, 0, :],
                                        ALU.subtract).then_inc(s_rest, 1)

            def split_third(k):
                dve.wait_ge(s_part1, k + 1)
                dve.wait_ge(s_rest, k + 1)
                nc.vector.tensor_tensor(parts[0:MP, k, 2, :], rest[0:MP, k % 2, :], parts[0:MP, k, 1, :],
                                        ALU.subtract).then_inc(s_part2, 1)

            def convert_ids(p):
                dve.wait_ge(s_idsb, (p + 1) * 16)
                past(dve, s_onehot, p * NM)
                nc.vector.tensor_copy(ids_h[:], ids_b[:]).then_inc(s_ids, 1)
                dve.wait_ge(s_ids, p + 1)

            def make_onehot(p, k):
                past(dve, emb_filled, (p - 1) * EMB_JOBS + JOB_OF[k] + 1)
                for c in range(CH):
                    last = nc.vector.tensor_scalar(onehot[:, k, c, :], ids_h[:, k, :], row_of[:, c:c + 1], None,
                                                   ALU.is_equal)
                last.then_inc(s_onehot, 1)

            def move_lookup(p, k):
                dve.wait_ge(emb_filled, p * EMB_JOBS + k + 1)
                nc.vector.tensor_copy(*lookup_views(k)).then_inc(emb_dve, 1)

            def move_rows(p, t, k):
                dve.wait_ge(emb_filled, p * EMB_JOBS + LOOK + t * NT + k + 1)
                nc.vector.tensor_copy(*row_views(t, k)).then_inc(emb_dve, 1)

            def keep_blocks(p, t, s):
                step = t * STEPS + s
                dve.wait_ge(gram_filled, p * TILES * STEPS + step + 1)
                for q in range(Q):
                    last = nc.vector.tensor_copy(*block_views(t, s, q))
                last.then_inc(gram_dve, 1)

            def turn(p, t):
                dve.wait_ge(gram_dve, (p * TILES + t + 1) * (STEPS // 2))
                dve.wait_ge(gram_act, (p * TILES + t + 1) * (STEPS // 2))
                past(dve, s_z, (p - 1) * TILES + t + 1)
                nc.vector.transpose(turned[:, t, 0:NF * G], blocks[:, t, :, :].rearrange("p j g -> p (j g)")
                                    ).then_inc(s_turned, 1)
                dve.wait_ge(s_turned, p * TILES + t + 1)
                nc.vector.tensor_copy(turned[:, t, NF * 32:], turned[:, t, 0:SHIFTS * 32]).then_inc(s_ext, 1)
                dve.wait_ge(s_ext, p * TILES + t + 1)
                past(dve, mlp_filled, (p - 1) * MLP_JOBS + t + 1)
                src = sb_view(turned, t * JEXT * 32 + 32, [[33 * RUN, KCH], [32, SHIFTS], [33, RUN]])
                dst = z[:, t, :, 0:PAIRS_CH].rearrange("b c (s r) -> b c s r", r=RUN)
                nc.vector.tensor_copy(dst, src).then_inc(s_z, 1)

            dve.memset(embT[:, :, :, NF:], 0.0).then_inc(s_pad, 1)
            dve.memset(z[:, :, 1:, PAIRS_CH:], 0.0).then_inc(s_pad, 1)
            dve.wait_ge(s_rowi, 1)
            nc.vector.tensor_copy(row_of[:], row_of_i[:]).then_inc(s_row, 1)
            convert_ids(0)
            dve.wait_ge(s_row, 1)
            split_rest(0)
            for k in range(NM):
                if k + 1 < NM:
                    split_rest(k + 1)
                split_third(k)
                make_onehot(0, k)

            def body(p, first, last):
                if not first:
                    for f in LK[-1]:
                        make_onehot(p, f)
                if not last:
                    convert_ids(p + 1)
                for k in range(LOOK):
                    if k % 2:
                        move_lookup(p, k)
                    if not last and k < LOOK - 1:
                        for f in LK[k]:
                            make_onehot(p + 1, f)
                for t in range(TILES):
                    for k in range(NT):
                        if (LOOK + t * NT + k) % 2:
                            move_rows(p, t, k)
                    if t:
                        turn(p, 0)
                    for s in range(0, STEPS, 2):
                        keep_blocks(p, t, s)
                turn(p, 1)

            sweep(dve, body)

        @block.tensor
        def _(pe):
            def lookup(p, k):
                past(pe, (emb_act, emb_dve)[k % 2], p * (EMB_JOBS // 2) + k // 2)
                for m, f in enumerate(LK[k]):
                    pe.wait_ge(s_onehot, p * NM + f + 1)
                    if isinstance(p, int) and p == 0:
                        pe.wait_ge(s_part2, f + 1)
                        pe.wait_ge(s_part1, f + 1)
                    for c in range(CH):
                        for part in range(PARTS):
                            last = nc.tensor.matmul(emb_ps[k % 2][:, m * W:(m + 1) * W],
                                                    parts[0:MP, f, part, c * D:(c + 1) * D],
                                                    onehot[0:MP, f, c, :],
                                                    start=(c == 0 and part == 0),
                                                    stop=(c == CH - 1 and part == PARTS - 1))
                last.then_inc(emb_filled, 1)

            def transpose_rows(p, t, k):
                job = LOOK + t * NT + k
                past(pe, (emb_act, emb_dve)[job % 2], p * (EMB_JOBS // 2) + job // 2)
                pe.wait_ge(s_rows[t][k], (p + 1) * 16 * len(TR[k]))
                for m, n in enumerate(TR[k]):
                    last = nc.tensor.transpose(emb_ps[job % 2][:, m * P:(m + 1) * P], rows[:, t, n, :], ident[:])
                last.then_inc(emb_filled, 1)

            def gram(p, t, s):
                step = t * STEPS + s
                past(pe, (gram_dve, gram_act)[s % 2], p * (TILES * STEPS // 2) + step // 2)
                for g in range(GS):
                    four = embT[:, t, (GS * s + g) * Q:(GS * s + g + 1) * Q, :]
                    last = nc.tensor.matmul(gram_ps[s % 2][:, g // 4, (g % 4) * Q * NF:(g % 4 + 1) * Q * NF],
                                            four.rearrange("d q f -> d (q f)"), four[:, :, 0:NF],
                                            start=True, stop=True)
                last.then_inc(gram_filled, 1)

            def transpose_z(p, t):
                pe.wait_ge(s_z, p * TILES + t + 1)
                pe.wait_ge(s_ctx, (p + 1) * 16 * sum(n > 0 for n in CTX_CH))
                pe.wait_ge(mlp_moved, p * MLP_JOBS + t + 1)
                for c in range(KCH):
                    last = nc.tensor.transpose(mlp_ps[t][:, c * P:(c + 1) * P], z[:, t, c, :], ident[:])
                last.then_inc(mlp_filled, 1)

            def layers(p, step):
                base = p * MLP_JOBS
                if step == 0:
                    transpose_z(p, 1)
                elif step == 1:
                    pe.wait_ge(s_w1, 16 * KCH)
                    pe.wait_ge(s_const, 16 * 5)
                    for job in (2, 3):
                        pe.wait_ge(mlp_moved, BANKS + base + 2)
                        for m in range(2):
                            n = 2 * (job - 2) + m
                            for c in range(KCH):
                                last = nc.tensor.matmul(mlp_ps[job % 2][:, m * W:(m + 1) * W],
                                                        w1_sb[0:K1[c], c, n * P:(n + 1) * P], zT[0:K1[c], c, :],
                                                        start=(c == 0), stop=(c == KCH - 1))
                        last.then_inc(mlp_filled, 1)
                elif step == 2:
                    pe.wait_ge(mlp_moved, BANKS + base + 4)
                    for m in range(N2):
                        for n in range(N1):
                            last = nc.tensor.matmul(mlp_ps[0][:, m * W:(m + 1) * W],
                                                    w2_sb[:, n, m * P:(m + 1) * P], h1[:, n, :],
                                                    start=(n == 0), stop=(n == N1 - 1))
                    last.then_inc(mlp_filled, 1)
                else:
                    pe.wait_ge(mlp_moved, BANKS + base + 5)
                    for m in range(N2):
                        last = nc.tensor.matmul(mlp_ps[1][0:1, 0:W], w3_sb[:, m:m + 1], h2[:, m, :],
                                                start=(m == 0), stop=(m == N2 - 1))
                    last.then_inc(mlp_filled, 1)

            pe.wait_ge(s_const, 16 * 5)
            pe.wait_ge(s_pad, 1)

            def body(p, first, last):
                for k in range(LOOK):
                    lookup(p, k)
                    if not first and k < 3:
                        layers(p - 1, k)
                for t in range(TILES):
                    for k in range(NT):
                        transpose_rows(p, t, k)
                    if t == 0 and not first:
                        layers(p - 1, 3)
                    jobs = LOOK + (t + 1) * NT
                    pe.wait_ge(emb_act, p * (EMB_JOBS // 2) + (jobs + 1) // 2)
                    pe.wait_ge(emb_dve, p * (EMB_JOBS // 2) + jobs // 2)
                    for s in range(STEPS):
                        gram(p, t, s)
                transpose_z(p, 0)

            sweep(pe, body)
            for k in range(4):
                layers(PAIRS - 1, k)


def kernel(**inputs):
    import concourse.bacc as bacc
    from concourse.bass_utils import run_bass_kernel_spmd

    nc = bacc.Bacc("TRN2", target_bir_lowering=False, num_devices=1)
    arrays = {}

    def give(name, a):
        a = np.ascontiguousarray(a)
        arrays[name] = a
        return nc.dram_tensor(name, a.shape, mybir.dt.from_np(a.dtype), kind="ExternalInput").ap()

    ids_in = np.asarray(inputs["ids"]).reshape(B // P, Q, G, NF).transpose(0, 2, 1, 3).reshape(B, NF)
    ids = give("in_ids", ids_in)
    ids_mm = give("in_ids_mm", ids_in[:, MM_TABLES].T)
    w1_rows = give("in_w1_rows", first_layer_rows())
    ident = give("in_ident", np.eye(P, dtype=np.float32))
    dense_ctx = give("in_dense_ctx", inputs["dense_ctx"])
    tables = [give(f"in_tbl_{f}", inputs[f"tbl_{f}"]) for f in range(NF)]
    W1, b1, W2, b2, W3 = (give(f"in_{n}", inputs[n]) for n in ("W_top1", "b_top1", "W_top2", "b_top2", "W_top3"))
    out = nc.dram_tensor("out", (B, 1), F32, kind="ExternalOutput").ap()
    dlrm_tower(nc, ids, ids_mm, w1_rows, ident, dense_ctx, tables, W1, b1, W2, b2, W3, out)
    r = run_bass_kernel_spmd(nc, [arrays], core_ids=[0])
    return r.results[0]["out"]
```

```python
from contextlib import ExitStack

import numpy as np

import concourse.bass as bass
from concourse import mybir

F32 = mybir.dt.float32
F32R = mybir.dt.float32r
I32 = mybir.dt.int32
ALU = mybir.AluOpType
ACT = mybir.ActivationFunctionType

P = 128
B, NF, D, CTX = 2048, 27, 128, 16
H1, H2 = 512, 256
TILES = 2
PAIRS = B // (TILES * P)
W = TILES * P
SIZES = [1000, 1250, 1000, 1000, 1250, 1250, 125000, 12500, 1250, 12500, 1250, 1250, 1250, 1250,
         1250, 12500, 1000, 12500, 1000, 12500, 1000, 1250, 12500, 1000, 1000, 1000, 1000]

MM_ROWS, CH = 1000, 8
MP = MM_ROWS // CH
NM = 8
MM_TABLES = [f for f in range(NF) if SIZES[f] == MM_ROWS][:NM]
GATHERED = [f for f in range(NF) if f not in MM_TABLES]
NG = len(GATHERED)
SLOTS = GATHERED + MM_TABLES
PARTS = 2

STAGES = 4
OH = 4
ACT_ONEHOTS = (5, 7)
LOOK_TABLES, TR_TABLES = 2, 4
TR = [range(a, min(a + TR_TABLES, NG)) for a in range(0, NG, TR_TABLES)]
NT = len(TR)
LATE = range(NM - TR_TABLES, NM)


class Jobs:
    def __init__(self, look, look_by_dve, tr):
        self.look, self.tr, self.all = look, tr, look + TILES * tr
        self.bank = [k % 2 for k in range(look)] + TILES * [0, 2, 3, 4, 5, 1][:tr]
        self.by_dve = look_by_dve + TILES * [k % 2 for k in range(tr)]

    def after_tile(self, t):
        return range(self.look + (t + 1) * self.tr)


EVERY = Jobs(NM // LOOK_TABLES, [0, 1, 0, 0], NT)
FINAL = Jobs((NM - len(LATE)) // LOOK_TABLES, [0, 1], NT + 1)
DVE_JOBS = sum(EVERY.by_dve)
ACT_JOBS = EVERY.all - DVE_JOBS
NJ = NF - 1
Q, G = 4, 32
GS = 8
STEPS = G // GS
SHIFTS, RUN = NF // 2, 9
PAIRS_CH = SHIFTS * RUN
KCH = NF // RUN
CTX_CH = [P - PAIRS_CH, CTX - (P - PAIRS_CH), 0]
K1 = [PAIRS_CH + n for n in CTX_CH]
JEXT = NF + SHIFTS
SLOT = 32
GM = (Q - 1) * SLOT + NF
MLP_JOBS = 6
BANKS = 2
N1, N2 = H1 // P, H2 // P
LAST_LAYERS = [("z", 0), ("h1", 0), ("z", 1), ("h2", 0), ("h1", 1), ("y", 0), ("h2", 1), ("y", 1)]


def first_layer_rows():
    rows = []
    for c in range(KCH):
        for s in range(1, SHIFTS + 1):
            for r in range(RUN):
                i = c * RUN + r
                a, b = sorted((SLOTS[i], SLOTS[(i + s) % NF]))
                rows.append(b * (b - 1) // 2 + a)
        rows += [NF * (NF - 1) // 2 + sum(CTX_CH[:c]) + k for k in range(CTX_CH[c])]
    return rows


def dlrm_tower(nc, ids, ids_mm, ident_in, dense_ctx, tables, W1, b1, W2, b2, W3, out):
    with ExitStack() as ctx:
        def sb(name, shape, dt):
            return ctx.enter_context(nc.sbuf_tensor(name, shape, dt))

        def ps(name, shape):
            return ctx.enter_context(nc.psum_tensor(name, shape, F32))

        def sem(name):
            return ctx.enter_context(nc.semaphore(name))

        def sb_view(tile, first, dims, start=0, count=P):
            full = tile[:]
            pitch = full.ap[0][0]
            return bass.AP(full.tensor, start * pitch + first, [[pitch, count], *dims])

        ident = sb("ident", [P, P], F32)
        row_of = sb("row_of", [P, CH], F32)
        row_of_i = sb("row_of_i", [P, CH], I32)
        w1_sb = sb("w1_sb", [P, KCH, H1], F32)
        w2_sb = sb("w2_sb", [P, N1, H2], F32)
        w3_sb = sb("w3_sb", [P, N2], F32)
        b1_sb = sb("b1_sb", [P, N1], F32)
        b2_sb = sb("b2_sb", [P, N2], F32)
        parts = sb("parts", [P, NM, PARTS, CH * D], F32R)
        idx = sb("idx", [P, TILES, NF], I32)
        rows = sb("rows", [P, TILES, NG, D], F32)
        late_rows = sb("late_rows", [P, TILES, len(LATE), D], F32)
        ids_b = sb("ids_b", [P, NM, W], I32)
        ids_f = sb("ids_f", [P, NM, W], F32)
        onehot = sb("onehot", [P, OH, CH, W], F32R)
        embT = sb("embT", [P, TILES, P, SLOT], F32)
        blocks = sb("blocks", [P, TILES, NJ, G], F32)
        turned = sb("turned", [P, TILES, JEXT * 32], F32)
        z = sb("z", [P, TILES, KCH, P], F32)
        zT = sb("zT", [P, KCH, W], F32)
        h1 = sb("h1", [P, N1, W], F32)
        h2 = sb("h2", [P, N2, W], F32)
        y = sb("y", [1, W], F32)
        stage = [turned[:, t, 0:CH * D] for t in range(TILES)] + [
            sb_view(h1, 0, [[1, CH * D]]), sb_view(blocks, 0, [[1, CH * D]])]

        emb_ps = [ps(f"emb_ps{k}", [P, 512]) for k in range(2)]
        gram_ps = [ps(f"gram_ps{k}", [P, 2, 512]) for k in range(2)]
        mlp_ps = [ps(f"mlp_ps{k}", [P, 512]) for k in range(2)]

        s_const = sem("s_const")
        s_w1 = sem("s_w1")
        s_stage = [sem(f"s_stage{k}") for k in range(STAGES)]
        s_high = sem("s_high")
        s_low = sem("s_low")
        s_rowi = sem("s_rowi")
        s_row = sem("s_row")
        s_pad = sem("s_pad")
        s_idx = [sem(f"s_idx{t}") for t in range(TILES)]
        s_idsb = sem("s_idsb")
        s_ids_a = sem("s_ids_a")
        s_conv_a = sem("s_conv_a")
        s_ctx = sem("s_ctx")
        s_rows = [[sem(f"s_rows{t}_{k}") for k in range(NT)] for t in range(TILES)]
        s_late = [sem(f"s_late{t}") for t in range(TILES)]
        pool_waited = sem("pool_waited")
        sp_waited = sem("sp_waited")
        s_ids = sem("s_ids")
        s_onehot = sem("s_onehot")
        s_away = sem("s_away")
        onehot_act = sem("onehot_act")
        emb_filled = sem("emb_filled")
        emb_act = sem("emb_act")
        emb_dve = sem("emb_dve")
        gram_filled = sem("gram_filled")
        gram_dve = sem("gram_dve")
        gram_act = sem("gram_act")
        s_turned = sem("s_turned")
        s_ext = sem("s_ext")
        s_z = sem("s_z")
        mlp_filled = sem("mlp_filled")
        mlp_moved = sem("mlp_moved")
        s_out = sem("s_out")

        def past(eng, s, value):
            if not (isinstance(value, int) and value <= 0):
                eng.wait_ge(s, value)

        def sweep(eng, body):
            body(0, True, False)
            with eng.Fori(1, PAIRS - 1) as p:
                body(p, False, False)
            body(PAIRS - 1, False, True)

        def emb_bank(jobs, job):
            bank = jobs.bank[job]
            return emb_ps[bank][:] if bank < 2 else gram_ps[bank // 2 - 1][:, bank % 2, :]

        def wait_moved(eng, p, jobs, job):
            by_dve = sum(jobs.by_dve[:job + 1])
            if jobs.by_dve[job]:
                eng.wait_ge(emb_dve, p * DVE_JOBS + by_dve)
            else:
                eng.wait_ge(emb_act, p * ACT_JOBS + job + 1 - by_dve)

        def lookup_views(k):
            return (sb_view(embT, NG + LOOK_TABLES * k, [[1, LOOK_TABLES], [SLOT, W]]),
                    emb_ps[k % 2][:].rearrange("d (f b) -> d f b", f=LOOK_TABLES))

        def row_views(jobs, t, k):
            n, slot = (len(TR[k]), TR[k][0]) if k < NT else (len(LATE), NG + LATE[0])
            return (sb_view(embT, t * P * SLOT + slot, [[1, n], [SLOT, P]]),
                    emb_bank(jobs, jobs.look + t * jobs.tr + k)[:, 0:n * P].rearrange("d (f b) -> d f b", f=n))

        def block_views(t, s, q):
            src = gram_ps[s % 2][q * 32:q * 32 + NF, :, 0:4 * Q * NJ].rearrange("i h (g c) -> i h g c", g=4)
            return (sb_view(blocks, t * NJ * G + GS * s, [[4, 2], [1, 4], [G, NJ]], q * 32, NF),
                    src[:, :, :, q * NJ:(q + 1) * NJ])

        block = ctx.enter_context(nc.Block())

        @block.sync
        def _(sp):
            def load_ids(p):
                src = ids_mm[:, bass.ts(p, W)]
                sp.dma_start(ids_b[:], src.partition_broadcast(P)).then_inc(s_idsb, 16)

            def load_first_ids(a, b, landed):
                sp.dma_start(ids_b[:, a:b, :], ids_mm[a:b, 0:W].partition_broadcast(P)).then_inc(landed, 16)

            def load_idx(p, t):
                sp.dma_start(idx[:, t, :], ids[bass.ts(p * TILES + t, P), :]).then_inc(s_idx[t], 16)

            def load_table(k):
                src = tables[MM_TABLES[k]].rearrange("(p c) d -> p (c d)", c=CH)
                sp.dma_start(stage[k % STAGES][0:MP, :], src).then_inc(s_stage[k % STAGES], 16)

            def store_y(p):
                sp.dma_start(out[bass.ts(p, W), :].rearrange("n o -> o n"), y[:]).then_inc(s_out, 16)

            sp.sem_inc(s_out, 16)
            load_idx(0, 0)
            load_idx(0, 1)
            load_first_ids(0, 2, s_ids_a)
            load_table(0)
            load_table(1)
            load_first_ids(2, NM, s_idsb)
            load_table(2)
            load_table(3)
            for k in range(STAGES, NM):
                sp.wait_ge(s_high, k - STAGES + 1)
                sp.wait_ge(s_low, k - STAGES + 1)
                load_table(k)
            sp.dma_start(ident[:], ident_in).then_inc(s_const, 16)
            for c in range(KCH):
                at = sum(K1[:c])
                sp.dma_start(w1_sb[0:K1[c], c, :], W1[at:at + K1[c], :]).then_inc(s_w1, 16)
            sp.dma_start(w2_sb[:], W2.rearrange("(k p) n -> p k n", p=P)).then_inc(s_const, 16)
            with nc.allow_non_contiguous_dma(reason="short vectors, once"):
                sp.dma_start(w3_sb[:], W3.rearrange("(k p) n -> p (k n)", p=P)).then_inc(s_const, 16)
                sp.dma_start(b1_sb[:], b1.rearrange("(k p) -> p k", p=P)).then_inc(s_const, 16)
                sp.dma_start(b2_sb[:], b2.rearrange("(k p) -> p k", p=P)).then_inc(s_const, 16)

            def body(p, first, last):
                if not last:
                    sp.wait_ge(s_ids, p + 1)
                    load_ids(p + 1)
                if first:
                    sp.wait_ge(s_pad, 1)
                past(sp, mlp_filled, (p - 1) * MLP_JOBS + TILES)
                src = dense_ctx[bass.ts(p, W), :].rearrange("(t p) c -> p t c", p=P)
                for c in range(KCH):
                    if CTX_CH[c]:
                        at = sum(CTX_CH[:c])
                        sp.dma_start(z[:, :, c, PAIRS_CH:PAIRS_CH + CTX_CH[c]], src[:, :, at:at + CTX_CH[c]]
                                     ).then_inc(s_ctx, 16)
                if not last:
                    for t in range(TILES):
                        for k in range(NT):
                            sp.wait_ge(s_rows[t][k], (p + 1) * 16 * len(TR[k]))
                            sp.sem_inc(sp_waited, 1)
                        load_idx(p + 1, t)
                if not first:
                    sp.wait_ge(mlp_moved, BANKS + p * MLP_JOBS)
                    store_y(p - 1)

            sweep(sp, body)
            sp.wait_ge(mlp_moved, BANKS + (PAIRS - 1) * MLP_JOBS + len(LAST_LAYERS))
            store_y(PAIRS - 1)
            sp.wait_ge(s_out, (PAIRS + 1) * 16)

        @block.gpsimd
        def _(pool):
            pool.iota(row_of_i[:], [[1, CH]], base=0, channel_multiplier=CH).then_inc(s_rowi, 1)

            def body(p, first, last):
                for t in range(TILES):
                    pool.wait_ge(s_idx[t], (p + 1) * 16)
                    for k in range(NT):
                        past(pool, emb_filled, (p - 1) * EVERY.all + EVERY.look + t * NT + k + 1)
                        pool.sem_inc(pool_waited, 1)
                        for n in TR[k]:
                            f = GATHERED[n]
                            pool.indirect_dma_start(rows[:, t, n, :], None, tables[f],
                                                    bass.IndirectOffsetOnAxis(idx[:, t, f:f + 1], 0)
                                                    ).then_inc(s_rows[t][k], 16)
                    if last:
                        for n, f in enumerate(LATE):
                            g = MM_TABLES[f]
                            pool.indirect_dma_start(late_rows[:, t, n, :], None, tables[g],
                                                    bass.IndirectOffsetOnAxis(idx[:, t, g:g + 1], 0)
                                                    ).then_inc(s_late[t], 16)

            sweep(pool, body)

        @block.scalar
        def _(act):
            def split_high(k):
                act.wait_ge(s_stage[k % STAGES], 16 * (k // STAGES + 1))
                nc.scalar.activation(parts[0:MP, k, 0, :], stage[k % STAGES][0:MP, :], ACT.Copy).then_inc(s_high, 1)

            def make_onehot(f):
                act.wait_ge(s_row, 1)
                act.wait_ge(s_ids, 1)
                act.wait_ge(emb_filled, (f - OH) // LOOK_TABLES + 1)
                for c in range(CH):
                    nc.scalar.activation(onehot[:, f % OH, c, :], ids_f[:, f, :], ACT.Abs,
                                         bias=row_of[:, c:c + 1], scale=-1.0).then_inc(s_away, 1)
                act.wait_ge(s_away, CH * (ACT_ONEHOTS.index(f) + 1))
                nc.scalar.activation(onehot[:, f % OH], onehot[:, f % OH].bitcast(F32), ACT.Relu,
                                     bias=1.0, scale=-1.0).then_inc(onehot_act, 1)

            def move_lookup(p, k):
                act.wait_ge(emb_filled, p * EVERY.all + k + 1)
                nc.scalar.activation(*lookup_views(k), ACT.Copy).then_inc(emb_act, 1)

            def move_rows(p, jobs, t, k):
                act.wait_ge(emb_filled, p * EVERY.all + jobs.look + t * jobs.tr + k + 1)
                nc.scalar.activation(*row_views(jobs, t, k), ACT.Copy).then_inc(emb_act, 1)

            def move_z(p, t):
                act.wait_ge(mlp_filled, p * MLP_JOBS + t + 1)
                nc.scalar.activation(zT[:, :, t * P:(t + 1) * P],
                                     mlp_ps[t][:, 0:KCH * P].rearrange("k (c b) -> k c b", c=KCH),
                                     ACT.Copy).then_inc(mlp_moved, 1)

            def bias_relu(dst, bias, p, job, ns):
                act.wait_ge(mlp_filled, p * MLP_JOBS + job + 1)
                for m, n in enumerate(ns):
                    last = nc.scalar.activation(dst[:, n, :], mlp_ps[job % 2][:, m * W:(m + 1) * W], ACT.Relu,
                                                bias=bias[:, n:n + 1])
                last.then_inc(mlp_moved, 1)

            def move_y(p):
                act.wait_ge(mlp_filled, (p + 1) * MLP_JOBS)
                act.wait_ge(s_out, (p + 1) * 16)
                nc.scalar.activation(y[:], mlp_ps[1][0:1, 0:W], ACT.Copy).then_inc(mlp_moved, 1)

            def keep_blocks(p, t, s):
                step = t * STEPS + s
                act.wait_ge(gram_filled, p * TILES * STEPS + step + 1)
                past(act, s_turned, (p - 1) * TILES + t + 1)
                for q in range(Q):
                    last = nc.scalar.activation(*block_views(t, s, q), ACT.Copy)
                last.then_inc(gram_act, 1)

            def last_layers(kind, t):
                job = LAST_LAYERS.index((kind, t))
                act.wait_ge(mlp_filled, (PAIRS - 1) * MLP_JOBS + job + 1)
                src, cols = mlp_ps[job % 2], bass.ts(t, P)
                if kind == "z":
                    done = nc.scalar.activation(zT[:, :, cols], src[:, 0:KCH * P].rearrange("k (c b) -> k c b", c=KCH),
                                                ACT.Copy)
                elif kind == "y":
                    if t == 0:
                        act.wait_ge(s_out, PAIRS * 16)
                    done = nc.scalar.activation(y[:, cols], src[0:1, 0:P], ACT.Copy)
                else:
                    dst, bias, count = (h1, b1_sb, N1) if kind == "h1" else (h2, b2_sb, N2)
                    for n in range(count):
                        done = nc.scalar.activation(dst[:, n, cols], src[:, bass.ts(n, P)], ACT.Relu,
                                                    bias=bias[:, n:n + 1])
                done.then_inc(mlp_moved, 1)

            def layers(p, step):
                if step == 0:
                    move_z(p, 1)
                elif step == 1:
                    act.wait_ge(s_const, 16 * 5)
                    bias_relu(h1, b1_sb, p, 2, (0, 1))
                    bias_relu(h1, b1_sb, p, 3, (2, 3))
                elif step == 2:
                    bias_relu(h2, b2_sb, p, 4, (0, 1))
                else:
                    move_y(p)

            act.sem_inc(mlp_moved, BANKS)
            for k in range(NM):
                if k == ACT_ONEHOTS[0]:
                    make_onehot(k)
                    move_lookup(0, 0)
                split_high(k)
            make_onehot(ACT_ONEHOTS[1])

            def body(p, first, last):
                jobs = FINAL if last else EVERY
                for k in range(EVERY.look):
                    if k < jobs.look and not jobs.by_dve[k] and not (first and k == 0):
                        move_lookup(p, k)
                    if not first and k < 2:
                        layers(p - 1, k)
                for t in range(TILES):
                    for k in range(jobs.tr):
                        if not jobs.by_dve[jobs.look + t * jobs.tr + k]:
                            move_rows(p, jobs, t, k)
                    if not first:
                        layers(p - 1, 2 + t)
                    for s in range(1, STEPS, 2):
                        if last and t and s == STEPS - 1:
                            last_layers("z", 0)
                        keep_blocks(p, t, s)
                if not last:
                    move_z(p, 0)

            sweep(act, body)
            for kind, t in LAST_LAYERS[1:]:
                last_layers(kind, t)

        @block.vector
        def _(dve):
            def split_low(k):
                dve.wait_ge(s_stage[k % STAGES], 16 * (k // STAGES + 1))
                dve.wait_ge(s_high, k + 1)
                nc.vector.tensor_tensor(parts[0:MP, k, 1, :], stage[k % STAGES][0:MP, :],
                                        parts[0:MP, k, 0, :].bitcast(F32), ALU.subtract).then_inc(s_low, 1)

            def convert_ids(p):
                dve.wait_ge(s_idsb, (p + 1) * 16)
                past(dve, s_onehot, p * NM - len(ACT_ONEHOTS))
                if isinstance(p, int) and p == 1:
                    dve.wait_ge(onehot_act, len(ACT_ONEHOTS))
                nc.vector.tensor_copy(ids_f[:], ids_b[:]).then_inc(s_ids, 1)
                dve.wait_ge(s_ids, p + 1)

            def make_onehot(p, k):
                if k >= OH:
                    dve.wait_ge(emb_filled, p * EVERY.all + (k - OH) // LOOK_TABLES + 1)
                else:
                    past(dve, emb_filled, (p - 1) * EVERY.all + (k + NM - OH) // LOOK_TABLES + 1)
                for c in range(CH):
                    last = nc.vector.tensor_scalar(onehot[:, k % OH, c, :], ids_f[:, k, :], row_of[:, c:c + 1], None,
                                                   ALU.is_equal)
                last.then_inc(s_onehot, 1)

            def move_lookup(p, k):
                dve.wait_ge(emb_filled, p * EVERY.all + k + 1)
                nc.vector.tensor_copy(*lookup_views(k)).then_inc(emb_dve, 1)

            def move_rows(p, jobs, t, k):
                dve.wait_ge(emb_filled, p * EVERY.all + jobs.look + t * jobs.tr + k + 1)
                nc.vector.tensor_copy(*row_views(jobs, t, k)).then_inc(emb_dve, 1)

            def keep_blocks(p, t, s):
                step = t * STEPS + s
                dve.wait_ge(gram_filled, p * TILES * STEPS + step + 1)
                for q in range(Q):
                    last = nc.vector.tensor_copy(*block_views(t, s, q))
                last.then_inc(gram_dve, 1)

            def turn(p, t):
                dve.wait_ge(gram_dve, (p * TILES + t + 1) * (STEPS // 2))
                dve.wait_ge(gram_act, (p * TILES + t + 1) * (STEPS // 2))
                past(dve, s_z, (p - 1) * TILES + t + 1)
                nc.vector.transpose(turned[:, t, 0:NJ * G], blocks[:, t, :, :].rearrange("p j g -> p (j g)")
                                    ).then_inc(s_turned, 1)
                dve.wait_ge(s_turned, p * TILES + t + 1)
                nc.vector.tensor_copy(turned[:, t, NF * 32:], turned[:, t, 0:SHIFTS * 32]).then_inc(s_ext, 1)
                base = t * JEXT * 32
                nc.vector.tensor_copy(sb_view(turned, base + NJ * 32 + NJ - SHIFTS, [[1, SHIFTS]]),
                                      sb_view(turned, base + (NJ - SHIFTS) * 32 + NJ, [[32, SHIFTS]])
                                      ).then_inc(s_ext, 1)
                dve.wait_ge(s_ext, (p * TILES + t + 1) * 2)
                past(dve, mlp_filled, (p - 1) * MLP_JOBS + t + 1)
                src = sb_view(turned, t * JEXT * 32 + 32, [[33 * RUN, KCH], [32, SHIFTS], [33, RUN]])
                dst = z[:, t, :, 0:PAIRS_CH].rearrange("b c (s r) -> b c s r", r=RUN)
                nc.vector.tensor_copy(dst, src).then_inc(s_z, 1)

            dve.memset(z[:, :, 1:, PAIRS_CH:], 0.0).then_inc(s_pad, 1)
            dve.wait_ge(s_rowi, 1)
            nc.vector.tensor_copy(row_of[:], row_of_i[:]).then_inc(s_row, 1)
            dve.memset(embT[:, :, :, NF:], 0.0).then_inc(s_pad, 1)
            dve.wait_ge(s_ids_a, 16)
            nc.vector.tensor_copy(ids_f[:, 0:2, :], ids_b[:, 0:2, :]).then_inc(s_conv_a, 1)
            dve.wait_ge(s_row, 1)
            dve.wait_ge(s_conv_a, 1)
            make_onehot(0, 0)
            split_low(0)
            make_onehot(0, 1)
            split_low(1)
            dve.wait_ge(s_idsb, 16)
            nc.vector.tensor_copy(ids_f[:, 2:, :], ids_b[:, 2:, :]).then_inc(s_ids, 1)
            dve.wait_ge(s_ids, 1)
            for k in range(2, NM):
                if k >= OH:
                    split_low(k)
                if k not in ACT_ONEHOTS:
                    make_onehot(0, k)
                if k < OH:
                    split_low(k)
                if k == LOOK_TABLES * 2:
                    move_lookup(0, 1)
            dve.wait_ge(s_low, NM)
            dve.memset(blocks[:], 0.0).then_inc(s_pad, 1)

            def body(p, first, last):
                jobs = FINAL if last else EVERY
                for k in range(EVERY.look):
                    if k < jobs.look and jobs.by_dve[k] and not first:
                        move_lookup(p, k)
                    if last:
                        continue
                    if not first and (k + 1) * LOOK_TABLES <= NM - OH:
                        for f in range(k * LOOK_TABLES, (k + 1) * LOOK_TABLES):
                            make_onehot(p, OH + f)
                    if k == 1:
                        convert_ids(p + 1)
                    if k == 2 and not first:
                        make_onehot(p + 1, 0)
                        make_onehot(p + 1, 1)
                for t in range(TILES):
                    for k in range(jobs.tr):
                        if jobs.by_dve[jobs.look + t * jobs.tr + k]:
                            move_rows(p, jobs, t, k)
                    if t:
                        turn(p, 0)
                    for s in range(0, STEPS, 2):
                        keep_blocks(p, t, s)
                        if first:
                            make_onehot(p + 1, (t * STEPS + s) // 2)
                        elif not last and s == 0:
                            make_onehot(p + 1, 2 + t)
                turn(p, 1)

            sweep(dve, body)

        @block.tensor
        def _(pe):
            def bank_free(p, jobs, job):
                bank = jobs.bank[job]
                if bank >= 2:
                    t = (job - jobs.look) // jobs.tr
                    past(pe, (gram_dve, gram_act)[bank // 2 - 1], (p * TILES + t) * (STEPS // 2))
                    return
                before = [j for j in range(job) if jobs.bank[j] == bank]
                if before:
                    wait_moved(pe, p, jobs, before[-1])
                elif not (isinstance(p, int) and p == 0):
                    wait_moved(pe, p - 1, EVERY, max(j for j in range(EVERY.all) if EVERY.bank[j] == bank))

            def lookup(p, k):
                bank_free(p, EVERY, k)
                for m in range(LOOK_TABLES):
                    f = k * LOOK_TABLES + m
                    if isinstance(p, int) and p == 0:
                        pe.wait_ge(s_high, f + 1)
                        if f in ACT_ONEHOTS:
                            pe.wait_ge(onehot_act, ACT_ONEHOTS.index(f) + 1)
                        else:
                            pe.wait_ge(s_onehot, sum(k not in ACT_ONEHOTS for k in range(f + 1)))
                    else:
                        pe.wait_ge(s_onehot, p * NM - len(ACT_ONEHOTS) + f + 1)
                    for part in range(PARTS):
                        if part and isinstance(p, int) and p == 0:
                            pe.wait_ge(s_low, f + 1)
                        for c in range(CH):
                            last = nc.tensor.matmul(emb_ps[k % 2][:, m * W:(m + 1) * W],
                                                    parts[0:MP, f, part, c * D:(c + 1) * D],
                                                    onehot[0:MP, f % OH, c, :],
                                                    start=(c == 0 and part == 0),
                                                    stop=(c == CH - 1 and part == PARTS - 1))
                last.then_inc(emb_filled, 1)

            def transpose_rows(p, jobs, t, k):
                job = jobs.look + t * jobs.tr + k
                bank_free(p, jobs, job)
                if k < NT:
                    pe.wait_ge(s_rows[t][k], (p + 1) * 16 * len(TR[k]))
                    gathered = [rows[:, t, n, :] for n in TR[k]]
                else:
                    pe.wait_ge(s_late[t], 16 * len(LATE))
                    gathered = [late_rows[:, t, n, :] for n in range(len(LATE))]
                for m, table_rows in enumerate(gathered):
                    done = nc.tensor.transpose(emb_bank(jobs, job)[:, m * P:(m + 1) * P], table_rows, ident[:])
                done.then_inc(emb_filled, 1)

            def gram(p, t, s):
                step = t * STEPS + s
                past(pe, (gram_dve, gram_act)[s % 2], p * (TILES * STEPS // 2) + step // 2)
                for g in range(GS):
                    four = embT[:, t, (GS * s + g) * Q:(GS * s + g + 1) * Q, :]
                    last = nc.tensor.matmul(gram_ps[s % 2][0:GM, g // 4, (g % 4) * Q * NJ:(g % 4 + 1) * Q * NJ],
                                            four.rearrange("d q f -> d (q f)")[:, 0:GM], four[:, :, 0:NJ],
                                            start=True, stop=True)
                last.then_inc(gram_filled, 1)

            def transpose_z(p, t):
                pe.wait_ge(s_z, p * TILES + t + 1)
                pe.wait_ge(s_ctx, (p + 1) * 16 * sum(n > 0 for n in CTX_CH))
                pe.wait_ge(mlp_moved, p * MLP_JOBS + t + 1)
                for c in range(KCH):
                    last = nc.tensor.transpose(mlp_ps[t][:, c * P:(c + 1) * P], z[:, t, c, :], ident[:])
                last.then_inc(mlp_filled, 1)

            def layers(p, step):
                base = p * MLP_JOBS
                if step == 0:
                    transpose_z(p, 1)
                elif step == 1:
                    pe.wait_ge(s_w1, 16 * KCH)
                    pe.wait_ge(s_const, 16 * 5)
                    for job in (2, 3):
                        pe.wait_ge(mlp_moved, BANKS + base + 2)
                        for m in range(2):
                            n = 2 * (job - 2) + m
                            for c in range(KCH):
                                last = nc.tensor.matmul(mlp_ps[job % 2][:, m * W:(m + 1) * W],
                                                        w1_sb[0:K1[c], c, n * P:(n + 1) * P], zT[0:K1[c], c, :],
                                                        start=(c == 0), stop=(c == KCH - 1))
                        last.then_inc(mlp_filled, 1)
                elif step == 2:
                    pe.wait_ge(mlp_moved, BANKS + base + 4)
                    for m in range(N2):
                        for n in range(N1):
                            last = nc.tensor.matmul(mlp_ps[0][:, m * W:(m + 1) * W],
                                                    w2_sb[:, n, m * P:(m + 1) * P], h1[:, n, :],
                                                    start=(n == 0), stop=(n == N1 - 1))
                    last.then_inc(mlp_filled, 1)
                else:
                    pe.wait_ge(mlp_moved, BANKS + base + 5)
                    for m in range(N2):
                        last = nc.tensor.matmul(mlp_ps[1][0:1, 0:W], w3_sb[:, m:m + 1], h2[:, m, :],
                                                start=(m == 0), stop=(m == N2 - 1))
                    last.then_inc(mlp_filled, 1)

            def last_layers(kind, t):
                job, cols = LAST_LAYERS.index((kind, t)), bass.ts(t, P)
                dst = mlp_ps[job % 2]
                source = {"h1": "z", "h2": "h1", "y": "h2"}.get(kind)
                before = max(job - BANKS, LAST_LAYERS.index((source, t)) if source else job - BANKS)
                pe.wait_ge(mlp_moved, BANKS + (PAIRS - 1) * MLP_JOBS + before + 1)
                if kind == "z":
                    pe.wait_ge(s_z, (PAIRS - 1) * TILES + t + 1)
                    if t == 0:
                        pe.wait_ge(s_ctx, PAIRS * 16 * sum(n > 0 for n in CTX_CH))
                    for c in range(KCH):
                        done = nc.tensor.transpose(dst[:, c * P:(c + 1) * P], z[:, t, c, :], ident[:])
                elif kind == "h1":
                    for n in range(N1):
                        for c in range(KCH):
                            done = nc.tensor.matmul(dst[:, bass.ts(n, P)], w1_sb[0:K1[c], c, n * P:(n + 1) * P],
                                                    zT[0:K1[c], c, cols], start=(c == 0), stop=(c == KCH - 1))
                elif kind == "h2":
                    for m in range(N2):
                        for n in range(N1):
                            done = nc.tensor.matmul(dst[:, bass.ts(m, P)], w2_sb[:, n, m * P:(m + 1) * P],
                                                    h1[:, n, cols], start=(n == 0), stop=(n == N1 - 1))
                else:
                    for m in range(N2):
                        done = nc.tensor.matmul(dst[0:1, 0:P], w3_sb[:, m:m + 1], h2[:, m, cols],
                                                start=(m == 0), stop=(m == N2 - 1))
                done.then_inc(mlp_filled, 1)

            def body(p, first, last):
                jobs = FINAL if last else EVERY
                for k in range(EVERY.look):
                    if k < jobs.look:
                        lookup(p, k)
                    if not first and k < 2:
                        layers(p - 1, k)
                if first:
                    pe.wait_ge(s_const, 16 * 5)
                    pe.wait_ge(s_pad, 3)
                for t in range(TILES):
                    for k in range(jobs.tr):
                        transpose_rows(p, jobs, t, k)
                    if not first:
                        layers(p - 1, 2 + t)
                    wait_moved(pe, p, jobs, max(j for j in jobs.after_tile(t) if jobs.by_dve[j]))
                    wait_moved(pe, p, jobs, max(j for j in jobs.after_tile(t) if not jobs.by_dve[j]))
                    for s in range(STEPS):
                        if last and t and s == STEPS - 1:
                            last_layers("z", 0)
                        gram(p, t, s)
                if not last:
                    transpose_z(p, 0)

            sweep(pe, body)
            for kind, t in LAST_LAYERS[1:]:
                last_layers(kind, t)


def kernel(**inputs):
    import concourse.bacc as bacc
    from concourse.bass_utils import run_bass_kernel_spmd

    nc = bacc.Bacc("TRN2", target_bir_lowering=False, num_devices=1)
    arrays = {}

    def give(name, a):
        a = np.ascontiguousarray(a)
        arrays[name] = a
        return nc.dram_tensor(name, a.shape, mybir.dt.from_np(a.dtype), kind="ExternalInput").ap()

    ids_in = np.asarray(inputs["ids"]).reshape(B // P, Q, G, NF).transpose(0, 2, 1, 3).reshape(B, NF)
    ids = give("in_ids", ids_in)
    ids_mm = give("in_ids_mm", ids_in[:, MM_TABLES].T)
    ident = give("in_ident", np.eye(P, dtype=np.float32))
    dense_ctx = give("in_dense_ctx", inputs["dense_ctx"])
    tables = [give(f"in_tbl_{f}", inputs[f"tbl_{f}"]) for f in range(NF)]
    W1 = give("in_W_top1", np.asarray(inputs["W_top1"])[first_layer_rows()])
    b1, W2, b2, W3 = (give(f"in_{n}", inputs[n]) for n in ("b_top1", "W_top2", "b_top2", "W_top3"))
    out = nc.dram_tensor("out", (B, 1), F32, kind="ExternalOutput").ap()
    dlrm_tower(nc, ids, ids_mm, ident, dense_ctx, tables, W1, b1, W2, b2, W3, out)
    r = run_bass_kernel_spmd(nc, [arrays], core_ids=[0])
    return r.results[0]["out"]
```
